# Optimizing a Trainium2 kernel written in Bass

```python
import numpy as np
import jax
import jax.numpy as jnp

def _softmax(x, axis=-1):
    return jax.nn.softmax(x, axis=axis)

def _gelu(x):
    return jax.nn.gelu(x, approximate=True)

def _silu(x):
    return jax.nn.silu(x)

def _sigmoid(x):
    return jax.nn.sigmoid(x)

def _layernorm(x, axis=-1, eps=1e-05):
    m = jnp.mean(x, axis=axis, keepdims=True)
    v = jnp.var(x, axis=axis, keepdims=True)
    return (x - m) / jnp.sqrt(v + eps)

def _scatter_add(tgt, idx, src, axis=0):
    return tgt.at[idx].add(src)

def _segment_sum(src, seg, n):
    return jax.ops.segment_sum(src, seg, n)
kernel_name = 'mk_adj_resnorm_d1_adj_r2_8c29f2'

def setup_inputs(seed: int=0):
    np.random.seed(seed)
    _w = jnp.asarray

    def _rec_inputs():
        import jax
        import jax.numpy as jnp
        _gk = jax.random.key(seed)
        x = -0.000929 + 1 * jax.random.normal(jax.random.fold_in(_gk, 1), (1354, 128), jnp.float32)
        _a = jax.random.bernoulli(jax.random.fold_in(_gk, 2), 0.00295421, (1354, 1354))
        _af = _a.astype(jnp.float32)
        adj = _af
        return (x, adj)
    x, adj = _rec_inputs()

    def _L0_gnn_setup():
        import jax, jax.numpy as jnp
        import numpy as np
        N = 4096
        F_IN = 128
        FILTERS = 128
        EDGE_PROB = 0.004
        key = jax.random.key(seed)
        k_x, k_a, k_w1, k_w2, k_w3 = jax.random.split(key, 5)
        x = jax.random.normal(k_x, (N, F_IN), dtype=jnp.float32)
        A = (jax.random.uniform(k_a, (N, N)) < EDGE_PROB).astype(jnp.float32)
        scale = 1.0 / np.sqrt(F_IN)
        W1 = jax.random.normal(k_w1, (F_IN, FILTERS), dtype=jnp.float32) * scale
        W2 = jax.random.normal(k_w2, (F_IN, FILTERS), dtype=jnp.float32) * scale
        W3 = jax.random.normal(k_w3, (F_IN, FILTERS), dtype=jnp.float32) * scale
        return {'x': x, 'A': A, 'W1': W1, 'W2': W2, 'W3': W3}
    _L0_gnn_all = _L0_gnn_setup()
    _L0_gnn_in = {k: v for k, v in _L0_gnn_all.items() if k in ('W1', 'W2', 'W3')}
    del _L0_gnn_all
    return {'x': x, 'adj': adj, 'L0_gnn_W1': _L0_gnn_in['W1'], 'L0_gnn_W2': _L0_gnn_in['W2'], 'L0_gnn_W3': _L0_gnn_in['W3']}

def reference(x, adj, L0_gnn_W1, L0_gnn_W2, L0_gnn_W3):
    import jax
    import jax.numpy as jnp

    def _L0_gnn_ref(x, A, W1, W2, W3):
        import jax, jax.numpy as jnp
        import numpy as np
        N = 4096
        F_IN = 128
        FILTERS = 128
        EDGE_PROB = 0.004
        A2 = A @ A
        A3 = A2 @ A
        f1 = A @ x @ W1
        f2 = A2 @ x @ W2
        f3 = A3 @ x @ W3
        return (f1 + f2 + f3) / 3.0
    x = _layernorm(x + _L0_gnn_ref(x, adj, L0_gnn_W1, L0_gnn_W2, L0_gnn_W3), axis=-1)
    return x

_drawn_inputs = setup_inputs


def setup_inputs(seed=0):
    import zlib

    import numpy as np

    out = dict(_drawn_inputs(seed))
    spreads = {}
    factors = {}
    for name, (base, spread) in spreads.items():
        noise = np.random.default_rng([zlib.crc32(name.encode()), seed]).standard_normal(out[name].shape)
        drawn = base * np.exp(spread * noise) if base else spread * noise
        out[name] = jnp.asarray(drawn.astype(out[name].dtype))
    for name, factor in factors.items():
        out[name] = (out[name] * factor).astype(out[name].dtype)
    return out
```

```python
from contextlib import ExitStack

import concourse.bass as bass
from concourse import mybir

F32 = mybir.dt.float32
F32R = mybir.dt.float32r
BF16 = mybir.dt.bfloat16
U16 = mybir.dt.uint16
I32 = mybir.dt.int32
ALU = mybir.AluOpType
ACT = mybir.ActivationFunctionType
AX = mybir.AxisListType

P = 128
Q = 32
G = P // Q
EPS = 1e-5
LEAD = 3



def gnn_resnorm(nc: bass.Bass, x: bass.AP, adj: bass.AP, w1: bass.AP, w2: bass.AP, w3: bass.AP, out: bass.AP):
    N, F = x.shape
    T = -(-N // (G * Q))
    SPAN = T * Q
    TAIL = N - (G - 1) * SPAN
    TF = TAIL // Q
    REST = TAIL - TF * Q
    assert F == P and 0 < REST and TF < T

    with ExitStack() as ctx:
        def sb(name, shape, dt):
            return ctx.enter_context(nc.sbuf_tensor(name, shape, dt))

        def sem(name):
            return ctx.enter_context(nc.semaphore(name))

        NS = 2
        a_nat = sb("a_nat", [P, T, G, SPAN], F32)
        a_t = sb("a_t", [P, T, T, P], F32R)
        a_turned = sb("a_turned", [P, NS, T, P], F32)
        x_sb = sb("x_sb", [P, T, F], F32)
        x_t = sb("x_t", [P, T, P], F32)
        w_sb = sb("w_sb", [P, 3, F], F32)
        xw = sb("xw", [P, T, 3, F], F32)
        v_even = sb("v_even", [P, T, 2, F], F32R)
        v_odd = sb("v_odd", [P, T, 2, F], F32R)
        v = [v_even, v_odd, v_even]
        ident = sb("ident", [P, P], F32)
        ones = sb("ones", [P, 1], F32)
        warm = sb("warm", [P, 512], BF16)
        eps = sb("eps", [P, 1], F32)
        u_sb = sb("u_sb", [P, 4, F], F32)
        t_sb = sb("t_sb", [P, 4, F], F32)
        y_sb = sb("y_sb", [P, T, F], F32)
        stats = sb("stats", [P, T, 6], F32)
        moments = sb("moments", [P, T, 2], F32)
        std = sb("std", [P, T], F32)
        rstd = sb("rstd", [P, T], F32)
        low_out = sb("low_out", [P, G * SPAN], BF16)
        low_sum = sb("low_sum", [P, T], F32)
        low_all = sb("low_all", [P, 1], F32)
        flag = sb("flag", [1, 1], I32)
        a_stage = a_turned[:, 0, :, :]
        a_rows = a_turned[:, 1, :, :].rearrange("p s m -> p (s m)")

        bank = [ctx.enter_context(nc.psum_tensor(f"bank{i}", [P, 512], F32)) for i in range(8)]
        xt_ps = bank[0:2]
        xw_ps = bank[2:4]
        mm_ps = bank[4:8]
        NB = len(mm_ps)

        warm_ready, ident_ready, pads_ready, consts_ready = map(sem, ("warm_ready", "ident_ready", "pads_ready", "consts_ready"))
        XG = [(0, 4), (4, 8), (8, T)]
        x_in = [sem(f"x_in{i}") for i in range(len(XG))]
        x_in_cnt = [0] * len(XG)
        w_in = sem("w_in")
        a_in = [sem(f"a_in{t}") for t in range(T)]
        xt_done, xt_ready, xw_done, xw_ready, high0, low0 = map(sem, ("xt_done", "xt_ready", "xw_done", "xw_ready", "high0", "low0"))
        at_turned, at_ready, mm_done, part_ready, sum_ready, high_ready, low_ready = map(
            sem, ("at_turned", "at_ready", "mm_done", "part_ready", "sum_ready", "high_ready", "low_ready"))
        lowsum_ready, lowall_ready, flag_done, flag_ready = map(sem, ("lowsum_ready", "lowall_ready", "flag_done", "flag_ready"))
        stats_ready, mom_ready, std_ready, rstd_ready, o_ready, out_done = map(
            sem, ("stats_ready", "mom_ready", "std_ready", "rstd_ready", "o_ready", "out_done"))

        x_dmas = [[] for _ in XG]
        for i, (a, b) in enumerate(XG):
            for g in range(G):
                e = b if g < G - 1 else min(b, TF)
                if e > a:
                    x_dmas[i].append((x_sb[g * Q:(g + 1) * Q, a:e, :],
                                      x[g * SPAN + a * Q:g * SPAN + e * Q, :].rearrange("(t c) f -> c t f", c=Q)))
            if a <= TF < b:
                x_dmas[i].append((x_sb[(G - 1) * Q:(G - 1) * Q + REST, TF, :], x[N - REST:N, :]))

        def a_dmas(t):
            got = []
            for g in range(G):
                w = SPAN if g < G - 1 else TAIL
                hs = G if t < TF else G - 1
                rows = adj[0:(G - 1) * SPAN, g * SPAN:g * SPAN + w].rearrange("(h n) j -> n h j", h=G - 1)
                if hs == G:
                    for_all = bass.AP(tensor=adj.tensor, offset=adj.offset + t * Q * N + g * SPAN,
                                      ap=[[N, Q], [SPAN * N, G], [1, w]])
                    got.append((a_nat[g * Q:(g + 1) * Q, t, :, 0:w], for_all))
                else:
                    got.append((a_nat[g * Q:(g + 1) * Q, t, 0:hs, 0:w], rows[t * Q:(t + 1) * Q]))
                if t == TF:
                    got.append((a_nat[g * Q:g * Q + REST, t, G - 1, 0:w],
                                adj[N - REST:N, g * SPAN:g * SPAN + w]))
            return got

        OG = [(0, 3), (3, 6), (6, 8), (8, TF), (TF, TF + 1)] + [(t, t + 1) for t in range(TF + 1, T)]
        out_dmas = []
        for a, b in OG:
            for g in range(G):
                if g == G - 1 and a > TF:
                    continue
                if g == G - 1 and a == TF:
                    out_dmas.append((b, out[N - REST:N, :], y_sb[g * Q:g * Q + REST, a, :]))
                    continue
                out_dmas.append((b, out[g * SPAN + a * Q:g * SPAN + b * Q, :].rearrange("(t c) f -> c t f", c=Q),
                                 y_sb[g * Q:(g + 1) * Q, a:b, :]))

        g_rows, g_at, g_mm, g_sum = map(sem, ("g_rows", "g_at", "g_mm", "g_sum"))

        early = {4: 0, 7: 1, T - 1: 2}
        assert len(early) == LEAD
        checks = {T + 1 + (3 * k) // 2: k for k in range(T)}
        FLAG_AT = max(checks) + 1
        assert len(checks) == T and FLAG_AT + 2 < 3 * T

        block = ctx.enter_context(nc.Block())

        @block.sync
        def _(sp):
            for i in range(len(XG)):
                for dst, src in x_dmas[i]:
                    if dst.shape[0] == REST:
                        sp.wait_ge(pads_ready, 1)
                    sp.dma_start(dst, src).then_inc(x_in[i], 16)
            for t in range(T):
                for dst, src in a_dmas(t):
                    if dst.shape[0] == REST:
                        sp.wait_ge(pads_ready, 2)
                    sp.dma_start(dst, src).then_inc(a_in[t], 16)
            for need, dst, src in out_dmas:
                sp.wait_ge(o_ready, need)
                sp.dma_start(dst, src).then_inc(out_done, 16)
            sp.wait_ge(out_done, 16 * len(out_dmas))
            sp.wait_ge(flag_ready, 1)
            general = sp.value_load(flag[0:1, 0:1], min_val=0, max_val=1)
            with sp.If(general > 0):
                sp.wait_ge(o_ready, 2 * T)
                for _, dst, src in out_dmas:
                    sp.dma_start(dst, src).then_inc(out_done, 16)
                sp.wait_ge(out_done, 32 * len(out_dmas))

        @block.gpsimd
        def _(pool):
            nc.gpsimd.memset(x_sb[(G - 1) * Q:, TF:, :], 0.0).then_inc(pads_ready, 1)
            pool.wait_ge(pads_ready, 1)
            nc.gpsimd.memset(a_nat[:, TF:, G - 1, :], 0.0).then_inc(pads_ready, 1)
            pool.wait_ge(pads_ready, 2)
            nc.gpsimd.memset(ident[:], 0.0).then_inc(ident_ready, 1)
            pool.wait_ge(ident_ready, 1)
            nc.gpsimd.affine_select(out=ident[:], in_=ident[:], compare_op=ALU.not_equal, fill=1.0, base=0,
                                    pattern=[[-1, P]], channel_multiplier=1).then_inc(ident_ready, 1)
            pool.wait_ge(ident_ready, 2)
            nc.gpsimd.memset(a_nat[(G - 1) * Q:, 0:TF, :, TAIL:], 0.0).then_inc(pads_ready, 1)
            pool.wait_ge(pads_ready, 3)
            nc.gpsimd.memset(a_nat[(G - 1) * Q:, TF:, 0:G - 1, TAIL:], 0.0).then_inc(pads_ready, 1)
            pool.wait_ge(pads_ready, 4)
            for k in range(T):
                pool.wait_ge(high0, k + 1)
                nc.gpsimd.tensor_tensor(v[0][:, k, 1, :], xw[:, k, 2, :], v[0][:, k, 0, :].bitcast(F32),
                                        ALU.subtract).then_inc(low0, 1)
            for n in range(2 * T):
                p, t = divmod(n, T)
                pool.wait_ge(high_ready, n + 1)
                nc.gpsimd.tensor_tensor(v[p + 1][:, t, 1, :], u_sb[:, n % 4, :], v[p + 1][:, t, 0, :].bitcast(F32),
                                        ALU.subtract).then_inc(low_ready, 1)

        @block.scalar
        def _(act):
            for i, w in enumerate((w1, w2, w3)):
                act.dma_start(w_sb[:, i, :], w).then_inc(w_in, 16)

            def store_at(t):
                act.wait_ge(at_turned, t + 1)
                nc.scalar.activation(a_t[:, t, :, :], a_turned[:, t % NS, :, :], ACT.Copy).then_inc(at_ready, 1)

            def check_low(t):
                if t:
                    act.wait_ge(lowsum_ready, t)
                lows = a_nat[:, t, :, :].rearrange("p h j -> p (h j)").bitcast(U16)[:, 0:2 * G * SPAN:2]
                nc.scalar.activation(low_out[:, :], lows, ACT.Copy,
                                     accum_out=low_sum[:, t:t + 1]).then_inc(lowsum_ready, 1)

            for i, (a, b) in enumerate(XG):
                act.wait_ge(xt_done, i + 1)
                nc.scalar.activation(x_t[:, a:b, :], xt_ps[i % 2][:, 0:(b - a) * P].rearrange("p (t n) -> p t n", n=P),
                                     ACT.Copy).then_inc(xt_ready, 1)
                for k in range(a, b):
                    act.wait_ge(xw_ready, k + 1)
                    nc.scalar.activation(v[0][:, k, 0, :], xw[:, k, 2, :], ACT.Copy).then_inc(high0, 1)
                    if k in early:
                        store_at(early[k])
            for n in range(2 * T):
                p, t = divmod(n, T)
                if p == 0 and t + LEAD < T:
                    store_at(t + LEAD)
                act.wait_ge(sum_ready, n + 1)
                if p == 1:
                    act.wait_ge(mm_done, T)
                nc.scalar.activation(v[p + 1][:, t, 0, :], u_sb[:, n % 4, :], ACT.Copy).then_inc(high_ready, 1)
                if n in checks:
                    check_low(checks[n])
            act.wait_ge(consts_ready, 1)
            for t in range(T):
                act.wait_ge(mom_ready, t + 1)
                nc.scalar.activation(std[:, t:t + 1], moments[:, t, 1:2], ACT.Sqrt, bias=eps[:, :]).then_inc(std_ready, 1)
                if 2 * T + t in checks:
                    check_low(checks[2 * T + t])
            act.wait_ge(flag_ready, 1)
            general = act.value_load(flag[0:1, 0:1], min_val=0, max_val=1)
            with act.If(general > 0):
                for t in range(T):
                    act.wait_ge(mom_ready, T + t + 1)
                    nc.scalar.activation(std[:, t:t + 1], moments[:, t, 1:2], ACT.Sqrt, bias=eps[:, :]).then_inc(std_ready, 1)

        @block.vector
        def _(dve):
            nc.vector.memset(warm[:], 0.0).then_inc(warm_ready, 1)
            nc.vector.memset(ones[:], 1.0).then_inc(consts_ready, 1)
            nc.vector.memset(eps[:], EPS).then_inc(consts_ready, 1)

            def transpose_a(t):
                dve.wait_ge(a_in[t], 16 * len(a_dmas(t)))
                dve.wait_ge(pads_ready, 4)
                if t >= NS:
                    dve.wait_ge(at_ready, t - NS + 1)
                nc.vector.transpose(a_turned[:, t % NS, :, :].rearrange("p s (h r) -> p h s r", r=Q),
                                    a_nat[:, t, :, :].rearrange("p h (s c) -> p h s c", c=Q)).then_inc(at_turned, 1)

            for k in range(T):
                dve.wait_ge(xw_done, k + 1)
                nc.vector.tensor_copy(xw[:, k, :, :], xw_ps[k % 2][:, 0:3 * F].rearrange("p (w f) -> p w f", f=F)
                                      ).then_inc(xw_ready, 1)
                if k in early:
                    transpose_a(early[k])

            def add_up(n):
                p, t = divmod(n, T)
                ps = mm_ps[n % NB]
                dve.wait_ge(mm_done, n + 1)
                if n >= 4:
                    dve.wait_ge(low_ready, n - 3)
                nc.vector.tensor_tensor(t_sb[:, n % 4, :], ps[:, F:2 * F], xw[:, t, 1 - p, :], ALU.add
                                        ).then_inc(part_ready, 1)
                dve.wait_ge(part_ready, n + 1)
                nc.vector.tensor_tensor(u_sb[:, n % 4, :], ps[:, 0:F], t_sb[:, n % 4, :], ALU.add
                                        ).then_inc(sum_ready, 1)

            for t in range(T):
                if t + LEAD < T:
                    transpose_a(t + LEAD)
                add_up(t)
            for t in range(T):
                add_up(T + t)

            def normalise(n):
                t = n % T
                dve.wait_ge(std_ready, n + 1)
                nc.vector.reciprocal(rstd[:, t:t + 1], std[:, t:t + 1]).then_inc(rstd_ready, 1)
                dve.wait_ge(rstd_ready, n + 1)
                nc.vector.tensor_scalar(y_sb[:, t, :], y_sb[:, t, :], moments[:, t, 0:1], rstd[:, t:t + 1],
                                        ALU.subtract, ALU.mult).then_inc(o_ready, 1)

            for t in range(T):
                n = 2 * T + t
                ps = mm_ps[n % NB]
                dve.wait_ge(mm_done, n + 1)
                nc.vector.scalar_tensor_tensor(t_sb[:, n % 4, :], ps[:, F:2 * F], 1.0 / 3.0, x_sb[:, t, :], ALU.mult, ALU.add
                                               ).then_inc(part_ready, 1)
                dve.wait_ge(part_ready, n + 1)
                nc.vector.scalar_tensor_tensor(y_sb[:, t, :], ps[:, 0:F], 1.0 / 3.0, t_sb[:, n % 4, :], ALU.mult, ALU.add
                                               ).then_inc(sum_ready, 1)
                dve.wait_ge(sum_ready, n + 1)
                nc.vector.bn_stats(stats[:, t, :], y_sb[:, t, :]).then_inc(stats_ready, 1)
                dve.wait_ge(stats_ready, t + 1)
                nc.vector.bn_aggr(moments[:, t, :], stats[:, t, :]).then_inc(mom_ready, 1)
                if t >= 1:
                    normalise(t - 1)
                if n == FLAG_AT:
                    dve.wait_ge(lowsum_ready, T)
                    nc.vector.tensor_reduce(low_all[:], low_sum[:], AX.X, ALU.add).then_inc(lowall_ready, 1)
                    dve.wait_ge(flag_done, 1)
                    nc.vector.tensor_scalar(flag[:], xt_ps[1][0:1, 0:1], 1.0, None, ALU.min).then_inc(flag_ready, 1)
            normalise(T - 1)

            general = dve.value_load(flag[0:1, 0:1], min_val=0, max_val=1)
            with dve.If(general > 0):
                dve.wait_ge(out_done, 16 * len(out_dmas))
                nc.vector.memset(low_all[:], 0.0).then_inc(g_sum, 1)
                for p in range(3):
                    with dve.Fori(0, T) as t:
                        n = p * T + t
                        nc.vector.tensor_copy(a_rows, a_nat[:, bass.ds(t, 1), :, :].rearrange("p o h j -> p (o h j)")
                                              ).then_inc(g_rows, 1)
                        dve.wait_ge(g_rows, n + 1)
                        nc.vector.transpose(a_stage.rearrange("p s (h r) -> p h s r", r=Q),
                                            a_rows.rearrange("p (h s c) -> p h s c", h=G, c=Q)).then_inc(g_at, 1)
                        dve.wait_ge(g_mm, n + 1)
                        if p < 2:
                            here = xw[:, bass.ds(t, 1), 1 - p, :]
                            nc.vector.tensor_tensor(here, mm_ps[0][:, 0:F], here, ALU.add).then_inc(g_sum, 1)
                        else:
                            nc.vector.scalar_tensor_tensor(y_sb[:, bass.ds(t, 1), :].rearrange("p o f -> p (o f)"),
                                                           mm_ps[0][:, 0:F], 1.0 / 3.0,
                                                           x_sb[:, bass.ds(t, 1), :].rearrange("p o f -> p (o f)"),
                                                           ALU.mult, ALU.add).then_inc(g_sum, 1)
                dve.wait_ge(g_sum, 3 * T + 1)
                for t in range(T):
                    nc.vector.bn_stats(stats[:, t, :], y_sb[:, t, :]).then_inc(stats_ready, 1)
                    dve.wait_ge(stats_ready, T + t + 1)
                    nc.vector.bn_aggr(moments[:, t, :], stats[:, t, :]).then_inc(mom_ready, 1)
                    normalise(T + t)

        @block.tensor
        def _(pe):
            pe.wait_ge(warm_ready, 1)
            for i in range(6):
                nc.tensor.matmul(mm_ps[i % NB][:, :], warm[:, 0:P], warm[:, :], start=True, stop=True)
            pe.wait_ge(ident_ready, 2)
            for i, (a, b) in enumerate(XG):
                pe.wait_ge(x_in[i], 16 * len(x_dmas[i]))
                if a <= TF < b:
                    pe.wait_ge(pads_ready, 1)
                if i >= 2:
                    pe.wait_ge(xt_ready, i - 1)
                for k in range(a, b):
                    mm = nc.tensor.transpose(xt_ps[i % 2][:, (k - a) * P:(k - a + 1) * P], x_sb[:, k, :], ident[:])
                mm.then_inc(xt_done, 1)
                if i == 0:
                    pe.wait_ge(w_in, 48)
                pe.wait_ge(xt_ready, i + 1)
                for k in range(a, b):
                    if k >= 2:
                        pe.wait_ge(xw_ready, k - 1)
                    nc.tensor.matmul(xw_ps[k % 2][:, 0:3 * F], x_t[:, k, :], w_sb[:, :, :].rearrange("p w f -> p (w f)"),
                                     start=True, stop=True).then_inc(xw_done, 1)
            pe.wait_ge(low0, T)
            for n in range(3 * T):
                p, t = divmod(n, T)
                if p == 0:
                    pe.wait_ge(at_ready, t + 1)
                if n >= NB:
                    pe.wait_ge(sum_ready, n - NB + 1)
                for s in range(T):
                    if p >= 1 and t == 0:
                        pe.wait_ge(low_ready, (p - 1) * T + s + 1)
                    mm = nc.tensor.matmul(mm_ps[n % NB][:, 0:2 * F], a_t[:, t, s, :],
                                          v[p][:, s, :, :].rearrange("p h f -> p (h f)"),
                                          start=(s == 0), stop=(s == T - 1))
                mm.then_inc(mm_done, 1)
                if n == FLAG_AT + 2:
                    pe.wait_ge(consts_ready, 1)
                    pe.wait_ge(lowall_ready, 1)
                    nc.tensor.matmul(xt_ps[1][0:1, 0:1], low_all[:], ones[:], start=True, stop=True).then_inc(flag_done, 1)
            pe.wait_ge(flag_ready, 1)
            general = pe.value_load(flag[0:1, 0:1], min_val=0, max_val=1)
            with pe.If(general > 0):
                for p in range(3):
                    rhs = xw[:, :, 2 - p, :]
                    pe.wait_ge(g_sum, p * T + 1)
                    with pe.Fori(0, T) as t:
                        n = p * T + t
                        pe.wait_ge(g_at, n + 1)
                        pe.wait_ge(g_sum, n + 1)
                        for s in range(T):
                            mm = nc.tensor.matmul(mm_ps[0][:, 0:F], a_stage[:, s, :], rhs[:, s, :],
                                                  start=(s == 0), stop=(s == T - 1))
                        mm.then_inc(g_mm, 1)


_INS = ["x", "adj", "L0_gnn_W1", "L0_gnn_W2", "L0_gnn_W3"]


def kernel(**inputs):
    import numpy as _np
    import concourse.bacc as _bacc
    from concourse import mybir as _mybir
    from concourse.bass_utils import run_bass_kernel_spmd as _run

    nc = _bacc.Bacc("TRN2", target_bir_lowering=False, num_devices=1)
    arrays, args = {}, []
    for name in _INS:
        a = _np.ascontiguousarray(inputs[name])
        arrays[f"in_{name}_dram"] = a
        args.append(nc.dram_tensor(f"in_{name}_dram", a.shape, _mybir.dt.from_np(a.dtype), kind="ExternalInput").ap())
    shape = inputs["x"].shape
    args.append(nc.dram_tensor("out_0_dram", shape, _mybir.dt.float32, kind="ExternalOutput").ap())
    gnn_resnorm(nc, *args)
    r = _run(nc, [arrays], core_ids=[0])
    return r.results[0]["out_0_dram"]
```

```python
from contextlib import ExitStack

import concourse.bass as bass
from concourse import mybir

F32 = mybir.dt.float32
F32R = mybir.dt.float32r
BF16 = mybir.dt.bfloat16
U16 = mybir.dt.uint16
I32 = mybir.dt.int32
ALU = mybir.AluOpType
ACT = mybir.ActivationFunctionType
AX = mybir.AxisListType

P = 128
Q = 32
G = P // Q
EPS = 1e-5
LEAD = 2
WARM = 10
SLOTS = 4



def gnn_resnorm(nc: bass.Bass, x: bass.AP, adj: bass.AP, w1: bass.AP, w2: bass.AP, w3: bass.AP, out: bass.AP):
    N, F = x.shape
    T = -(-N // (G * Q))
    SPAN = T * Q
    TAIL = N - (G - 1) * SPAN
    TF = TAIL // Q
    REST = TAIL - TF * Q
    assert F == P and 0 < REST and TF < T

    with ExitStack() as ctx:
        def sb(name, shape, dt):
            return ctx.enter_context(nc.sbuf_tensor(name, shape, dt))

        def sem(name):
            return ctx.enter_context(nc.semaphore(name))

        a_nat = sb("a_nat", [P, T, G, SPAN], F32)
        NT = 2
        a_turned = sb("a_turned", [P, NT, T, P], F32)
        a_t = sb("a_t", [P, T, T, P], F32R)
        x_sb = sb("x_sb", [P, T, F], F32)
        x_t = sb("x_t", [P, T, 2, P], F32R)
        w_sb = sb("w_sb", [P, 3, F], F32)
        w_pair = sb("w_pair", [P, 3, 2, F], F32R)
        v_even = sb("v_even", [P, T, 2, F], F32R)
        v_odd = sb("v_odd", [P, T, 2, F], F32R)
        v = [v_even, v_odd, v_even]
        ident = sb("ident", [P, P], F32)
        ones = sb("ones", [P, 1], F32)
        warm = sb("warm", [P, 512], BF16)
        eps = sb("eps", [P, 1], F32)
        t_sb = sb("t_sb", [P, SLOTS, F], F32)
        u_sb = sb("u_sb", [P, SLOTS, F], F32)
        y_sb = sb("y_sb", [P, T, F], F32)
        stats = sb("stats", [P, T, 6], F32)
        moments = sb("moments", [P, T, 2], F32)
        std = sb("std", [P, T], F32)
        rstd = sb("rstd", [P, T], F32)
        low_out = sb("low_out", [P, G * SPAN], BF16)
        low_sum = sb("low_sum", [P, T], F32)
        low_all = sb("low_all", [P, 1], F32)
        flag = sb("flag", [1, 1], I32)
        g_factor = [sb(f"g_factor{i}", [P, T, F], F32) for i in range(2)]
        g_xt = sb("g_xt", [P, 2, P], F32R)
        a_stage = a_turned[:, 0, :, :]
        a_rows = a_turned[:, 1, :, :].rearrange("p s m -> p (s m)")

        bank = [ctx.enter_context(nc.psum_tensor(f"bank{i}", [P, 512], F32)) for i in range(8)]
        XB = 4
        XG = [(a, min(a + XB, T)) for a in range(0, T, XB)]
        assert len(XG) == 3
        xt_ps = [bank[0], bank[1], bank[2]]
        v0_ps = [bank[3], bank[0], bank[1]]

        def bank_of(n):
            return 4 + n % 4 if n < T else (n - T) % 8

        last_user = {}
        previous = []
        for n in range(3 * T):
            previous.append(last_user.get(bank_of(n)))
            last_user[bank_of(n)] = n

        order = []
        AHEAD = 4
        SPARE = 7
        begun = [0] * AHEAD
        for t in range(T):
            order.append((t, 0, T))
            left = SPARE
            for i in range(AHEAD):
                more = min(t - 1 - begun[i], left) if i <= t < T - 1 else 0
                if more > 0:
                    order.append((T + i, begun[i], begun[i] + more))
                    begun[i] += more
                    left -= more
        order += [(T + i, begun[i], T - 1) for i in range(AHEAD)] + [(T + AHEAD, 0, T - 1)]
        order += [(T + i, T - 1, T) for i in range(AHEAD + 1)]
        order += [(n, 0, T) for n in range(T + AHEAD + 1, 2 * T)]
        order += [(2 * T + i, 0, T - 1) for i in range(3)]
        order += [(2 * T + i, T - 1, T) for i in range(3)]
        order += [(n, 0, T) for n in range(2 * T + 3, 3 * T)]

        act_checks = dict(zip((T - 1, T + 1, T + 3, T + 5, 2 * T, 2 * T + 2), range(0, T, 2)))
        dve_checks = dict(zip((T - 3, T - 2, T, T + 2, T + 4), range(1, T, 2)))
        verdict = 2 * T + 4
        assert len(act_checks) + len(dve_checks) == T

        warm_ready, ident_ready, pads_ready, columns_ready, consts_ready = map(
            sem, ("warm_ready", "ident_ready", "pads_ready", "columns_ready", "consts_ready"))
        x_in, w3_in, w12_in, w_high, w_ready, w12_ready = map(
            sem, ("x_in", "w3_in", "w12_in", "w_high", "w_ready", "w12_ready"))
        a_rest_in = sem("a_rest_in")
        a_in = [sem(f"a_in{t}") for t in range(T)]
        xt_done, xt_high, xt_ready = map(sem, ("xt_done", "xt_high", "xt_ready"))
        v0_done, v0_high, v0_ready = map(sem, ("v0_done", "v0_high", "v0_ready"))
        at_turned, at_ready = map(sem, ("at_turned", "at_ready"))
        mm_done, part_ready, sum_ready, high_ready, low_ready = map(
            sem, ("mm_done", "part_ready", "sum_ready", "high_ready", "low_ready"))
        lowsum_act, lowsum_dve, lowall_ready, flag_done, flag_ready = map(sem, ("lowsum_act", "lowsum_dve", "lowall_ready", "flag_done", "flag_ready"))
        stats_ready, mom_ready, std_ready, rstd_ready, y_ready, sp_out_done, pool_out_done = map(
            sem, ("stats_ready", "mom_ready", "std_ready", "rstd_ready", "y_ready", "sp_out_done", "pool_out_done"))
        g_rows, g_at, g_x, g_mm, g_part, g_sum = map(sem, ("g_rows", "g_at", "g_x", "g_mm", "g_part", "g_sum"))

        x_dmas = []
        for g in range(G):
            e = T if g < G - 1 else TF
            x_dmas.append((x_sb[g * Q:(g + 1) * Q, 0:e, :],
                           x[g * SPAN:g * SPAN + e * Q, :].rearrange("(t c) f -> c t f", c=Q)))
        x_dmas.insert(1, (x_sb[(G - 1) * Q:(G - 1) * Q + REST, TF, :], x[N - REST:N, :]))

        def a_dmas(t):
            got = []
            for g in range(G):
                w = SPAN if g < G - 1 else TAIL
                hs = G if t < TF else G - 1
                rows = bass.AP(tensor=adj.tensor, offset=adj.offset + t * Q * N + g * SPAN,
                               ap=[[N, Q], [SPAN * N, hs], [1, w]])
                got.append((a_nat[g * Q:(g + 1) * Q, t, 0:hs, 0:w], rows))
            return got

        a_rest = []
        for g in range(G):
            w = SPAN if g < G - 1 else TAIL
            a_rest.append((a_nat[g * Q:g * Q + REST, TF, G - 1, 0:w], adj[N - REST:N, g * SPAN:g * SPAN + w]))

        def rows_out(g, a, b):
            return (b, out[g * SPAN + a * Q:g * SPAN + b * Q, :].rearrange("(t c) f -> c t f", c=Q),
                    y_sb[g * Q:(g + 1) * Q, a:b, :])

        sp_out = [rows_out(g, a, b) for a, b in ((0, 3), (3, 7)) for g in range(G - 1)]
        for t in range(7, T):
            rows = bass.AP(tensor=out.tensor, offset=out.offset + t * Q * F, ap=[[SPAN * F, G - 1], [F, Q], [1, F]])
            sp_out.append((t + 1, rows, y_sb[0:(G - 1) * Q, t, :]))
        pool_out = [rows_out(G - 1, a, b) for a, b in ((0, 3), (3, 7), (7, TF))]
        pool_out.append((TF + 1, out[N - REST:N, :], y_sb[(G - 1) * Q:(G - 1) * Q + REST, TF, :]))

        def in_bank(ps, k):
            return ps[:, 0:k * P].rearrange("p (t n) -> p t n", n=P)

        def low_words(t):
            return a_nat[:, t, :, :].rearrange("p h j -> p (h j)").bitcast(U16)[:, 0:2 * G * SPAN:2]

        block = ctx.enter_context(nc.Block())

        @block.sync
        def _(sp):
            for dst, src in x_dmas:
                if dst.shape[0] == REST:
                    sp.wait_ge(pads_ready, 1)
                sp.dma_start(dst, src).then_inc(x_in, 16)
            for t in range(T):
                for dst, src in a_dmas(t):
                    sp.dma_start(dst, src).then_inc(a_in[t], 16)
            for need, dst, src in sp_out:
                sp.wait_ge(y_ready, need)
                sp.dma_start(dst, src).then_inc(sp_out_done, 16)
            sp.wait_ge(flag_ready, 1)
            general = sp.value_load(flag[0:1, 0:1], min_val=0, max_val=1)
            with sp.If(general > 0):
                sp.wait_ge(y_ready, 2 * T)
                for _, dst, src in sp_out + pool_out:
                    sp.dma_start(dst, src).then_inc(sp_out_done, 16)
                sp.wait_ge(sp_out_done, 16 * (2 * len(sp_out) + len(pool_out)))
            sp.wait_ge(sp_out_done, 16 * len(sp_out))
            sp.wait_ge(pool_out_done, 16 * len(pool_out))

        @block.gpsimd
        def _(pool):
            nc.gpsimd.memset(x_sb[(G - 1) * Q:, TF:, :], 0.0).then_inc(pads_ready, 1)
            pool.wait_ge(pads_ready, 1)
            nc.gpsimd.memset(ident[:], 0.0).then_inc(ident_ready, 1)
            pool.wait_ge(ident_ready, 1)
            nc.gpsimd.affine_select(out=ident[:], in_=ident[:], compare_op=ALU.not_equal, fill=1.0, base=0,
                                    pattern=[[-1, P]], channel_multiplier=1).then_inc(ident_ready, 1)
            pool.wait_ge(ident_ready, 2)
            nc.gpsimd.memset(a_nat[:, TF:, G - 1, :], 0.0).then_inc(pads_ready, 1)
            pool.wait_ge(pads_ready, 2)
            for i, w in enumerate((w1, w2)):
                pool.dma_start(w_sb[:, i, :], w).then_inc(w12_in, 16)
            for dst, src in a_rest:
                pool.dma_start(dst, src).then_inc(a_rest_in, 16)
            pool.wait_ge(w_high, 2)
            pool.wait_ge(w12_in, 32)
            nc.gpsimd.tensor_tensor(w_pair[:, 0:2, 1, :], w_sb[:, 0:2, :], w_pair[:, 0:2, 0, :].bitcast(F32),
                                    ALU.subtract).then_inc(w12_ready, 1)
            for n in range(2 * T):
                p, t = divmod(n, T)
                pool.wait_ge(high_ready, n + 1)
                nc.gpsimd.tensor_tensor(v[p + 1][:, t, 1, :], u_sb[:, n % SLOTS, :], v[p + 1][:, t, 0, :].bitcast(F32),
                                        ALU.subtract).then_inc(low_ready, 1)
            for need, dst, src in pool_out:
                pool.wait_ge(y_ready, need)
                pool.dma_start(dst, src).then_inc(pool_out_done, 16)

        @block.scalar
        def _(act):
            act.dma_start(w_sb[:, 2, :], w3).then_inc(w3_in, 16)

            def store_at(t):
                act.wait_ge(at_turned, t + 1)
                nc.scalar.activation(a_t[:, t, :, :], a_turned[:, t % NT, :, :], ACT.Copy).then_inc(at_ready, 1)

            def check_low(t):
                if t:
                    act.wait_ge(lowsum_act, t // 2)
                nc.scalar.activation(low_out[:, :], low_words(t), ACT.Copy,
                                     accum_out=low_sum[:, t:t + 1]).then_inc(lowsum_act, 1)

            act.wait_ge(consts_ready, 1)
            nc.scalar.activation(std[:, 0:1], eps[:, :], ACT.Sqrt)
            act.wait_ge(w3_in, 16)
            nc.scalar.activation(w_pair[:, 2, 0, :], w_sb[:, 2, :], ACT.Copy).then_inc(w_high, 1)
            for i, (a, b) in enumerate(XG):
                act.wait_ge(xt_done, i + 1)
                nc.scalar.activation(x_t[:, a:b, 0, :], in_bank(xt_ps[i], b - a), ACT.Copy).then_inc(xt_high, 1)
            for i, (a, b) in enumerate(XG):
                act.wait_ge(v0_done, i + 1)
                nc.scalar.activation(v[0][:, a:b, 0, :], in_bank(v0_ps[i], b - a), ACT.Copy).then_inc(v0_high, 1)
                if i == 0:
                    act.wait_ge(w12_in, 32)
                    nc.scalar.activation(w_pair[:, 0:2, 0, :], w_sb[:, 0:2, :], ACT.Copy).then_inc(w_high, 1)
                    store_at(0)
            for t in range(1, LEAD):
                store_at(t)

            def high(n):
                p, t = divmod(n, T)
                act.wait_ge(sum_ready, n + 1)
                if p == 1:
                    act.wait_ge(mm_done, T)
                nc.scalar.activation(v[p + 1][:, t, 0, :], u_sb[:, n % SLOTS, :], ACT.Copy).then_inc(high_ready, 1)

            for n in range(2 * T):
                if n in act_checks:
                    check_low(act_checks[n])
                if n + LEAD < T:
                    store_at(n + LEAD)
                high(n)

            def root(n):
                t = n % T
                act.wait_ge(mom_ready, n + 1)
                nc.scalar.activation(std[:, t:t + 1], moments[:, t, 1:2], ACT.Sqrt, bias=eps[:, :]).then_inc(std_ready, 1)

            for t in range(T):
                root(t)
                if 2 * T + t in act_checks:
                    check_low(act_checks[2 * T + t])
            act.wait_ge(flag_ready, 1)
            general = act.value_load(flag[0:1, 0:1], min_val=0, max_val=1)
            with act.If(general > 0):
                for t in range(T):
                    root(T + t)

        @block.vector
        def _(dve):
            nc.vector.memset(warm[:], 0.0).then_inc(warm_ready, 1)
            nc.vector.memset(eps[:], EPS).then_inc(consts_ready, 1)
            nc.vector.memset(ones[:], 1.0).then_inc(consts_ready, 1)

            nc.vector.memset(a_nat[(G - 1) * Q:, 0:TF, :, TAIL:], 0.0).then_inc(columns_ready, 1)
            nc.vector.memset(a_nat[(G - 1) * Q:, TF:, 0:G - 1, TAIL:], 0.0).then_inc(columns_ready, 1)

            def turn_a(t):
                dve.wait_ge(a_in[t], 16 * G)
                if t == TF:
                    dve.wait_ge(a_rest_in, 16 * len(a_rest))
                dve.wait_ge(pads_ready, 2)
                dve.wait_ge(columns_ready, 2)
                if t >= NT:
                    dve.wait_ge(at_ready, t - NT + 1)
                nc.vector.transpose(a_turned[:, t % NT, :, :].rearrange("p s (h r) -> p h s r", r=Q),
                                    a_nat[:, t, :, :].rearrange("p h (s c) -> p h s c", c=Q)).then_inc(at_turned, 1)

            dve.wait_ge(w_high, 1)
            nc.vector.tensor_tensor(w_pair[:, 2, 1, :], w_sb[:, 2, :], w_pair[:, 2, 0, :].bitcast(F32),
                                    ALU.subtract).then_inc(w_ready, 1)
            for i, (a, b) in enumerate(XG):
                dve.wait_ge(xt_high, i + 1)
                nc.vector.tensor_tensor(x_t[:, a:b, 1, :], in_bank(xt_ps[i], b - a), x_t[:, a:b, 0, :].bitcast(F32),
                                        ALU.subtract).then_inc(xt_ready, 1)
            turn_a(0)
            for i, (a, b) in enumerate(XG):
                dve.wait_ge(v0_high, i + 1)
                nc.vector.tensor_tensor(v[0][:, a:b, 1, :], in_bank(v0_ps[i], b - a), v[0][:, a:b, 0, :].bitcast(F32),
                                        ALU.subtract).then_inc(v0_ready, 1)
                if i == 0:
                    turn_a(1)
            for t in range(2, LEAD):
                turn_a(t)

            def add_up(n):
                dve.wait_ge(mm_done, n + 1)
                if n >= SLOTS:
                    dve.wait_ge(low_ready, n - SLOTS + 1)
                nc.vector.tensor_reduce(u_sb[:, n % SLOTS, :], bank[bank_of(n)][:, 0:2 * F].rearrange("p (h f) -> p f h", h=2),
                                        AX.X, ALU.add).then_inc(sum_ready, 1)

            for n in range(2 * T):
                if n + LEAD < T and n == 0:
                    turn_a(LEAD)
                add_up(n)
                if n + LEAD + 1 < T:
                    turn_a(n + LEAD + 1)
                if n in dve_checks:
                    t = dve_checks[n]
                    nc.vector.tensor_reduce(low_sum[:, t:t + 1], low_words(t), AX.X, ALU.max).then_inc(lowsum_dve, 1)

            def invert(n):
                t = n % T
                dve.wait_ge(std_ready, n + 1)
                nc.vector.reciprocal(rstd[:, t:t + 1], std[:, t:t + 1]).then_inc(rstd_ready, 1)

            def normalise(n):
                t = n % T
                dve.wait_ge(rstd_ready, n + 1)
                nc.vector.tensor_scalar(y_sb[:, t, :], y_sb[:, t, :], moments[:, t, 0:1], rstd[:, t:t + 1],
                                        ALU.subtract, ALU.mult).then_inc(y_ready, 1)

            def third_of_low(t):
                n = 2 * T + t
                dve.wait_ge(mm_done, n + 1)
                dve.wait_ge(sum_ready, n - SLOTS + 1)
                nc.vector.scalar_tensor_tensor(t_sb[:, n % SLOTS, :], bank[bank_of(n)][:, F:2 * F], 1.0 / 3.0, x_sb[:, t, :],
                                               ALU.mult, ALU.add).then_inc(part_ready, 1)

            def third_of_high(t):
                n = 2 * T + t
                dve.wait_ge(part_ready, t + 1)
                nc.vector.scalar_tensor_tensor(y_sb[:, t, :], bank[bank_of(n)][:, 0:F], 1.0 / 3.0, t_sb[:, n % SLOTS, :],
                                               ALU.mult, ALU.add).then_inc(sum_ready, 1)

            def take_stats(t):
                dve.wait_ge(sum_ready, 2 * T + t + 1)
                nc.vector.bn_stats(stats[:, t, :], y_sb[:, t, :]).then_inc(stats_ready, 1)

            def take_moments(t):
                dve.wait_ge(stats_ready, t + 1)
                nc.vector.bn_aggr(moments[:, t, :], stats[:, t, :]).then_inc(mom_ready, 1)

            for t in range(T + 2):
                if t < T:
                    third_of_low(t)
                if t >= 2:
                    invert(t - 2)
                if 1 <= t <= T:
                    take_stats(t - 1)
                if t < T:
                    third_of_high(t)
                if 1 <= t <= T:
                    take_moments(t - 1)
                if t >= 2:
                    normalise(t - 2)
                if 2 * T + t == verdict:
                    dve.wait_ge(lowsum_act, len(act_checks))
                    dve.wait_ge(lowsum_dve, len(dve_checks))
                    nc.vector.tensor_reduce(low_all[:], low_sum[:], AX.X, ALU.add).then_inc(lowall_ready, 1)
                if t == T:
                    dve.wait_ge(flag_done, 1)
                    nc.vector.tensor_scalar(flag[:], bank[bank_of(verdict + 1)][0:1, 511:512], 1.0, None, ALU.min
                                            ).then_inc(flag_ready, 1)

            general = dve.value_load(flag[0:1, 0:1], min_val=0, max_val=1)
            with dve.If(general > 0):
                dve.wait_ge(sp_out_done, 16 * len(sp_out))
                dve.wait_ge(pool_out_done, 16 * len(pool_out))
                nc.vector.memset(low_all[:], 0.0).then_inc(g_sum, 1)
                for q in range(4):
                    with dve.Fori(0, T) as t:
                        m = q * T + t
                        if q < 3:
                            nc.vector.tensor_copy(g_xt[:, :, :], x_t[:, bass.ds(t, 1), :, :].rearrange(
                                "p o h n -> p (o h) n").bitcast(F32)).then_inc(g_x, 1)
                        if q >= 1:
                            nc.vector.tensor_copy(a_rows, a_nat[:, bass.ds(t, 1), :, :].rearrange("p o h j -> p (o h j)")
                                                  ).then_inc(g_rows, 1)
                            dve.wait_ge(g_rows, m - T + 1)
                            nc.vector.transpose(a_stage.rearrange("p s (h r) -> p h s r", r=Q),
                                                a_rows.rearrange("p (h s c) -> p h s c", h=G, c=Q)).then_inc(g_at, 1)
                        dve.wait_ge(g_mm, m + 1)
                        if q < 3:
                            nc.vector.tensor_copy(t_sb[:, 0, :], bank[0][:, F:2 * F]).then_inc(g_part, 1)
                            dve.wait_ge(g_part, m + 1)
                            nc.vector.tensor_tensor(g_factor[q % 2][:, bass.ds(t, 1), :].rearrange("p o f -> p (o f)"),
                                                    bank[0][:, 0:F], t_sb[:, 0, :], ALU.add).then_inc(g_sum, 1)
                        else:
                            nc.vector.scalar_tensor_tensor(y_sb[:, bass.ds(t, 1), :].rearrange("p o f -> p (o f)"),
                                                           bank[0][:, 0:F], 1.0 / 3.0,
                                                           x_sb[:, bass.ds(t, 1), :].rearrange("p o f -> p (o f)"),
                                                           ALU.mult, ALU.add).then_inc(g_sum, 1)
                dve.wait_ge(g_sum, 4 * T + 1)
                for t in range(T):
                    nc.vector.bn_stats(stats[:, t, :], y_sb[:, t, :]).then_inc(stats_ready, 1)
                    dve.wait_ge(stats_ready, T + t + 1)
                    nc.vector.bn_aggr(moments[:, t, :], stats[:, t, :]).then_inc(mom_ready, 1)
                    invert(T + t)
                    normalise(T + t)

        @block.tensor
        def _(pe):
            pe.wait_ge(warm_ready, 1)
            for i in range(WARM):
                nc.tensor.matmul(bank[4 + i % 4][:, :], warm[:, 0:P], warm[:, :], start=True, stop=True)
            pe.wait_ge(ident_ready, 2)
            pe.wait_ge(pads_ready, 1)
            pe.wait_ge(x_in, 16 * len(x_dmas))

            for i, (a, b) in enumerate(XG):
                for k in range(a, b):
                    mm = nc.tensor.transpose(xt_ps[i][:, (k - a) * P:(k - a + 1) * P], x_sb[:, k, :], ident[:])
                mm.then_inc(xt_done, 1)

            def times_w(ps, t, w, stop):
                nc.tensor.matmul(ps, x_t[:, t, 0, :], w_pair[:, w, :, :].rearrange("p h f -> p (h f)"), start=True, stop=False)
                return nc.tensor.matmul(ps, x_t[:, t, 1, :], w_pair[:, w, :, :].rearrange("p h f -> p (h f)"),
                                        start=False, stop=stop)

            pe.wait_ge(w_ready, 1)
            for i, (a, b) in enumerate(XG):
                pe.wait_ge(xt_ready, i + 1)
                if i:
                    pe.wait_ge(xt_ready, 2)
                for t in range(a, b):
                    for h in range(4):
                        mm = nc.tensor.matmul(v0_ps[i][:, (t - a) * F:(t - a + 1) * F], x_t[:, t, h // 2, :],
                                              w_pair[:, 2, h % 2, :], start=(h == 0), stop=(h == 3))
                mm.then_inc(v0_done, 1)
            pe.wait_ge(w12_ready, 1)
            for n in range(4):
                times_w(bank[bank_of(n)][:, 0:2 * F], n, 1, False)

            factor_waits = [0] * 3
            for n, s0, s1 in order:
                p, t = divmod(n, T)
                ps = bank[bank_of(n)][:, 0:2 * F]
                if s0 == 0:
                    if previous[n] is not None:
                        pe.wait_ge(sum_ready, previous[n] + 1)
                    elif n >= T:
                        pe.wait_ge(v0_ready, len(XG))
                    if 4 <= n < 2 * T:
                        times_w(ps, t, 1 - p, False)
                if p == 0:
                    pe.wait_ge(at_ready, t + 1)
                for s in range(s0, s1):
                    if s >= factor_waits[p]:
                        factor_waits[p] = s + 1
                        if p == 0:
                            pe.wait_ge(v0_ready, s // XB + 1)
                        else:
                            pe.wait_ge(low_ready, (p - 1) * T + s + 1)
                    mm = nc.tensor.matmul(ps, a_t[:, t, s, :], v[p][:, s, :, :].rearrange("p h f -> p (h f)"),
                                          start=(p == 2 and s == 0), stop=(s == T - 1))
                if s1 == T:
                    mm.then_inc(mm_done, 1)
                if n == 3 * T - 2:
                    pe.wait_ge(consts_ready, 2)
                    pe.wait_ge(lowall_ready, 1)
                    pe.wait_ge(sum_ready, verdict + 2)
                    nc.tensor.matmul(bank[bank_of(verdict + 1)][0:1, 511:512], low_all[:], ones[:],
                                     start=True, stop=True).then_inc(flag_done, 1)

            pe.wait_ge(flag_ready, 1)
            general = pe.value_load(flag[0:1, 0:1], min_val=0, max_val=1)
            with pe.If(general > 0):
                ps = bank[0]
                for q in range(4):
                    pe.wait_ge(g_sum, q * T + 1)
                    with pe.Fori(0, T) as t:
                        m = q * T + t
                        pe.wait_ge(g_sum, m + 1)
                        if q < 3:
                            pe.wait_ge(g_x, m + 1)
                            for h in range(2):
                                mm = nc.tensor.matmul(ps[:, 0:2 * F], g_xt[:, h, :],
                                                      w_pair[:, 2 - q, :, :].rearrange("p h f -> p (h f)"),
                                                      start=(h == 0), stop=(q == 0 and h == 1))
                        if q >= 1:
                            pe.wait_ge(g_at, m - T + 1)
                            for s in range(T):
                                mm = nc.tensor.matmul(ps[:, 0:F], a_stage[:, s, :], g_factor[(q - 1) % 2][:, s, :],
                                                      start=(q == 3 and s == 0), stop=(s == T - 1))
                        mm.then_inc(g_mm, 1)


_INS = ["x", "adj", "L0_gnn_W1", "L0_gnn_W2", "L0_gnn_W3"]


def kernel(**inputs):
    import numpy as _np
    import concourse.bacc as _bacc
    from concourse import mybir as _mybir
    from concourse.bass_utils import run_bass_kernel_spmd as _run

    nc = _bacc.Bacc("TRN2", target_bir_lowering=False, num_devices=1)
    arrays, args = {}, []
    for name in _INS:
        a = _np.ascontiguousarray(inputs[name])
        arrays[f"in_{name}_dram"] = a
        args.append(nc.dram_tensor(f"in_{name}_dram", a.shape, _mybir.dt.from_np(a.dtype), kind="ExternalInput").ap())
    shape = inputs["x"].shape
    args.append(nc.dram_tensor("out_0_dram", shape, _mybir.dt.float32, kind="ExternalOutput").ap())
    gnn_resnorm(nc, *args)
    r = _run(nc, [arrays], core_ids=[0])
    return r.results[0]["out_0_dram"]
```

```python
from contextlib import ExitStack

import concourse.bass as bass
from concourse import mybir

F32 = mybir.dt.float32
F32R = mybir.dt.float32r
BF16 = mybir.dt.bfloat16
U16 = mybir.dt.uint16
I32 = mybir.dt.int32
ALU = mybir.AluOpType
ACT = mybir.ActivationFunctionType
AX = mybir.AxisListType

P = 128
Q = 32
G = P // Q
EPS = 1e-5
LEAD = 2
WARM = 8
SLOTS = 4



def gnn_resnorm(nc: bass.Bass, x: bass.AP, adj: bass.AP, w1: bass.AP, w2: bass.AP, w3: bass.AP, out: bass.AP):
    N, F = x.shape
    T = -(-N // (G * Q))
    SPAN = T * Q
    TAIL = N - (G - 1) * SPAN
    TF = TAIL // Q
    REST = TAIL - TF * Q
    assert F == P and 0 < REST and TF < T

    with ExitStack() as ctx:
        def sb(name, shape, dt):
            return ctx.enter_context(nc.sbuf_tensor(name, shape, dt))

        def sem(name):
            return ctx.enter_context(nc.semaphore(name))

        a_nat = sb("a_nat", [P, T, G, SPAN], F32)
        NT = 2
        a_turned = sb("a_turned", [P, NT, T, P], F32)
        a_t = sb("a_t", [P, T, T, P], F32R)
        x_sb = sb("x_sb", [P, T, F], F32)
        x_t = sb("x_t", [P, T, 2, P], F32R)
        w_sb = sb("w_sb", [P, 3, F], F32)
        w_pair = sb("w_pair", [P, 3, 2, F], F32R)
        v_even = sb("v_even", [P, T, 2, F], F32R)
        v_odd = sb("v_odd", [P, T, 2, F], F32R)
        v = [v_even, v_odd, v_even]
        ident = sb("ident", [P, P], F32)
        ones = sb("ones", [P, 1], F32)
        warm = sb("warm", [P, 512], BF16)
        eps = sb("eps", [P, 1], F32)
        u_sb = sb("u_sb", [P, SLOTS, F], F32)
        t_sb = sb("t_sb", [P, SLOTS, F], F32)
        y_sb = sb("y_sb", [P, T, F], F32)
        stats = sb("stats", [P, T, 6], F32)
        moments = sb("moments", [P, T, 2], F32)
        std = sb("std", [P, T], F32)
        rstd = sb("rstd", [P, T], F32)
        low_out = sb("low_out", [P, G // 2 * SPAN], BF16)
        low_sum = sb("low_sum", [P, 2 * T], F32)
        low_all = sb("low_all", [P, 1], F32)
        flag = sb("flag", [1, 1], I32)
        g_factor = [sb(f"g_factor{i}", [P, T, F], F32) for i in range(2)]
        g_xt = sb("g_xt", [P, 2, P], F32R)
        a_stage = a_turned[:, 0, :, :]
        a_rows = a_turned[:, 1, :, :].rearrange("p s m -> p (s m)")

        bank = [ctx.enter_context(nc.psum_tensor(f"bank{i}", [P, 512], F32)) for i in range(8)]
        XB = 4
        XG = [(a, min(a + XB, T)) for a in range(0, T, XB)]
        assert len(XG) == 3
        xt_ps = [bank[0], bank[1], bank[2]]
        v0_ps = [bank[3], bank[0], bank[1]]

        def bank_of(n):
            return 4 + n % 4 if n < T else (n - T) % 8

        last_user = {}
        previous = []
        for n in range(3 * T):
            previous.append(last_user.get(bank_of(n)))
            last_user[bank_of(n)] = n

        AHEAD = 4
        SPARE = 7
        BEFORE_LAST = 5
        order = [(t, -1, 0) for t in range(AHEAD)]
        begun = [0] * AHEAD
        for t in range(T):
            order.append((t, 0 if t < AHEAD else -1, T))
            if t == 1:
                order += [(T + i, -1, 0) for i in range(AHEAD)]
            left = SPARE
            for i in range(AHEAD):
                more = min(t - 1 - begun[i], left) if i <= t < T - 1 else 0
                if more > 0:
                    order.append((T + i, begun[i], begun[i] + more))
                    begun[i] += more
                    left -= more
        order += [(T + i, begun[i], T - 1) for i in range(AHEAD)]
        order += [(T + i, -1, T - 1) for i in range(AHEAD, BEFORE_LAST)]
        order += [(T + i, T - 1, T) for i in range(BEFORE_LAST)]
        order += [(n, -1, T) for n in range(T + BEFORE_LAST, 2 * T)]
        order += [(2 * T + i, -1, T - 1) for i in range(2)]
        order += [(2 * T + i, T - 1, T) for i in range(2)]
        order += [(n, -1, T) for n in range(2 * T + 2, 3 * T)]

        act_checks = [i for i in range(2 * T) if i % 4 < 2]
        dve_checks = [i for i in range(2 * T) if i % 4 >= 2]
        ACT_FROM, ACT_LAST = T - 1, 4
        DVE_FROM, DVE_LAST = T - 3, 3
        verdict = 2 * T + 7
        verdict_ps = bank[bank_of(3 * T)][0:1, 511:512]
        assert verdict < 3 * T - 1

        warm_ready, ident_ready, pads_ready, columns_ready, consts_ready = map(
            sem, ("warm_ready", "ident_ready", "pads_ready", "columns_ready", "consts_ready"))
        x_in, x_rest_in, w3_in, w12_in, w_high, w_ready, w12_ready = map(
            sem, ("x_in", "x_rest_in", "w3_in", "w12_in", "w_high", "w_ready", "w12_ready"))
        a_rest_in = sem("a_rest_in")
        a_in = [sem(f"a_in{t}") for t in range(T)]
        xt_done, xt_high, xt_ready = map(sem, ("xt_done", "xt_high", "xt_ready"))
        v0_done, v0_high, v0_ready = map(sem, ("v0_done", "v0_high", "v0_ready"))
        at_turned, at_ready = map(sem, ("at_turned", "at_ready"))
        mm_done, part_ready, sum_ready, high_ready, low_ready = map(
            sem, ("mm_done", "part_ready", "sum_ready", "high_ready", "low_ready"))
        lowsum_act, lowsum_dve, lowall_ready, flag_done, flag_ready = map(
            sem, ("lowsum_act", "lowsum_dve", "lowall_ready", "flag_done", "flag_ready"))
        stats_ready, mom_ready, std_ready, rstd_ready, y_ready, sp_out_done, pool_out_done = map(
            sem, ("stats_ready", "mom_ready", "std_ready", "rstd_ready", "y_ready", "sp_out_done", "pool_out_done"))
        g_rows, g_at, g_x, g_mm, g_part, g_sum = map(sem, ("g_rows", "g_at", "g_x", "g_mm", "g_part", "g_sum"))

        x_dmas = []
        for g in range(G):
            e = T if g < G - 1 else TF
            x_dmas.append((x_sb[g * Q:(g + 1) * Q, 0:e, :],
                           x[g * SPAN:g * SPAN + e * Q, :].rearrange("(t c) f -> c t f", c=Q)))

        def a_dmas(t):
            got = []
            for g in range(G):
                w = SPAN if g < G - 1 else TAIL
                hs = G if t < TF else G - 1
                rows = bass.AP(tensor=adj.tensor, offset=adj.offset + t * Q * N + g * SPAN,
                               ap=[[N, Q], [SPAN * N, hs], [1, w]])
                got.append((a_nat[g * Q:(g + 1) * Q, t, 0:hs, 0:w], rows))
            return got

        a_rest = []
        for g in range(G):
            w = SPAN if g < G - 1 else TAIL
            a_rest.append((a_nat[g * Q:g * Q + REST, TF, G - 1, 0:w], adj[N - REST:N, g * SPAN:g * SPAN + w]))

        CUTS = (0, 3, 7)
        def rows_out(g, a, b):
            return (b, out[g * SPAN + a * Q:g * SPAN + b * Q, :].rearrange("(t c) f -> c t f", c=Q),
                    y_sb[g * Q:(g + 1) * Q, a:b, :])

        sp_out = [rows_out(g, a, b) for a, b in zip(CUTS, CUTS[1:]) for g in range(G - 1)]
        for t in range(CUTS[-1], T):
            gs = G if t < TF else G - 1
            rows = bass.AP(tensor=out.tensor, offset=out.offset + t * Q * F, ap=[[SPAN * F, gs], [F, Q], [1, F]])
            sp_out.append((t + 1, rows, y_sb[0:gs * Q, t, :]))
        pool_out = [rows_out(G - 1, a, b) for a, b in zip(CUTS, CUTS[1:])]
        pool_out.append((TF + 1, out[N - REST:N, :], y_sb[(G - 1) * Q:(G - 1) * Q + REST, TF, :]))

        def in_bank(ps, k):
            return ps[:, 0:k * P].rearrange("p (t n) -> p t n", n=P)

        def low_words(i):
            h = i % 2 * (G // 2)
            return a_nat[:, i // 2, h:h + G // 2, :].rearrange("p h j -> p (h j)").bitcast(U16)[:, 0:G * SPAN:2]

        block = ctx.enter_context(nc.Block())

        @block.sync
        def _(sp):
            for dst, src in x_dmas:
                sp.dma_start(dst, src).then_inc(x_in, 16)
            sp.dma_start(w_sb[:, 2, :], w3).then_inc(w3_in, 16)
            for t in range(T):
                for dst, src in a_dmas(t):
                    sp.dma_start(dst, src).then_inc(a_in[t], 16)
            for need, dst, src in sp_out:
                sp.wait_ge(y_ready, need)
                sp.dma_start(dst, src).then_inc(sp_out_done, 16)
            sp.wait_ge(flag_ready, 1)
            general = sp.value_load(flag[0:1, 0:1], min_val=0, max_val=1)
            with sp.If(general > 0):
                sp.wait_ge(y_ready, 2 * T)
                for _, dst, src in sp_out + pool_out:
                    sp.dma_start(dst, src).then_inc(sp_out_done, 16)
                sp.wait_ge(sp_out_done, 16 * (2 * len(sp_out) + len(pool_out)))
            sp.wait_ge(sp_out_done, 16 * len(sp_out))
            sp.wait_ge(pool_out_done, 16 * len(pool_out))

        @block.gpsimd
        def _(pool):
            nc.gpsimd.memset(x_sb[(G - 1) * Q:, TF:, :], 0.0).then_inc(pads_ready, 1)
            pool.wait_ge(pads_ready, 1)
            pool.dma_start(x_sb[(G - 1) * Q:(G - 1) * Q + REST, TF, :], x[N - REST:N, :]).then_inc(x_rest_in, 16)
            nc.gpsimd.memset(ident[:], 0.0).then_inc(ident_ready, 1)
            pool.wait_ge(ident_ready, 1)
            nc.gpsimd.affine_select(out=ident[:], in_=ident[:], compare_op=ALU.not_equal, fill=1.0, base=0,
                                    pattern=[[-1, P]], channel_multiplier=1).then_inc(ident_ready, 1)
            pool.wait_ge(ident_ready, 2)
            nc.gpsimd.memset(a_nat[:, TF:, G - 1, :], 0.0).then_inc(pads_ready, 1)
            pool.wait_ge(pads_ready, 2)
            for i, w in enumerate((w1, w2)):
                pool.dma_start(w_sb[:, i, :], w).then_inc(w12_in, 16)
            for dst, src in a_rest:
                pool.dma_start(dst, src).then_inc(a_rest_in, 16)
            pool.wait_ge(w_high, 2)
            pool.wait_ge(w12_in, 32)
            nc.gpsimd.tensor_tensor(w_pair[:, 0:2, 1, :], w_sb[:, 0:2, :], w_pair[:, 0:2, 0, :].bitcast(F32),
                                    ALU.subtract).then_inc(w12_ready, 1)
            for n in range(2 * T):
                p, t = divmod(n, T)
                pool.wait_ge(high_ready, n + 1)
                nc.gpsimd.tensor_tensor(v[p + 1][:, t, 1, :], u_sb[:, n % SLOTS, :], v[p + 1][:, t, 0, :].bitcast(F32),
                                        ALU.subtract).then_inc(low_ready, 1)
            for need, dst, src in pool_out:
                pool.wait_ge(y_ready, need)
                pool.dma_start(dst, src).then_inc(pool_out_done, 16)

        @block.scalar
        def _(act):
            def store_at(t):
                act.wait_ge(at_turned, t + 1)
                nc.scalar.activation(a_t[:, t, :, :], a_turned[:, t % NT, :, :], ACT.Copy).then_inc(at_ready, 1)

            def check_low(k):
                if k:
                    act.wait_ge(lowsum_act, k)
                i = act_checks[k]
                nc.scalar.activation(low_out[:, :], low_words(i), ACT.Copy,
                                     accum_out=low_sum[:, i:i + 1]).then_inc(lowsum_act, 1)

            act.wait_ge(consts_ready, 1)
            nc.scalar.activation(std[:, 0:1], eps[:, :], ACT.Sqrt)
            act.wait_ge(w3_in, 16)
            nc.scalar.activation(w_pair[:, 2, 0, :], w_sb[:, 2, :], ACT.Copy).then_inc(w_high, 1)
            for i, (a, b) in enumerate(XG):
                act.wait_ge(xt_done, i + 1)
                nc.scalar.activation(x_t[:, a:b, 0, :], in_bank(xt_ps[i], b - a), ACT.Copy).then_inc(xt_high, 1)
            for i, (a, b) in enumerate(XG):
                act.wait_ge(v0_done, i + 1)
                nc.scalar.activation(v[0][:, a:b, 0, :], in_bank(v0_ps[i], b - a), ACT.Copy).then_inc(v0_high, 1)
                if i == 0:
                    act.wait_ge(w12_in, 32)
                    nc.scalar.activation(w_pair[:, 0:2, 0, :], w_sb[:, 0:2, :], ACT.Copy).then_inc(w_high, 1)
                    store_at(0)
            for t in range(1, LEAD):
                store_at(t)

            def high(n):
                p, t = divmod(n, T)
                act.wait_ge(sum_ready, n + 1)
                if p == 1:
                    act.wait_ge(mm_done, T)
                nc.scalar.activation(v[p + 1][:, t, 0, :], u_sb[:, n % SLOTS, :], ACT.Copy).then_inc(high_ready, 1)

            for n in range(2 * T):
                if 0 <= n - ACT_FROM < len(act_checks) - ACT_LAST:
                    check_low(n - ACT_FROM)
                if n + LEAD < T:
                    store_at(n + LEAD)
                high(n)

            def root(n):
                t = n % T
                act.wait_ge(mom_ready, n + 1)
                nc.scalar.activation(std[:, t:t + 1], moments[:, t, 1:2], ACT.Sqrt, bias=eps[:, :]).then_inc(std_ready, 1)

            for k in range(len(act_checks) - ACT_LAST, len(act_checks)):
                check_low(k)
            for t in range(T):
                root(t)
            act.wait_ge(flag_ready, 1)
            general = act.value_load(flag[0:1, 0:1], min_val=0, max_val=1)
            with act.If(general > 0):
                for t in range(T):
                    root(T + t)

        @block.vector
        def _(dve):
            nc.vector.memset(warm[:], 0.0).then_inc(warm_ready, 1)
            nc.vector.memset(eps[:], EPS).then_inc(consts_ready, 1)
            nc.vector.memset(ones[:], 1.0).then_inc(consts_ready, 1)

            nc.vector.memset(a_nat[(G - 1) * Q:, 0:TF, :, TAIL:], 0.0).then_inc(columns_ready, 1)
            nc.vector.memset(a_nat[(G - 1) * Q:, TF:, 0:G - 1, TAIL:], 0.0).then_inc(columns_ready, 1)

            def turn_a(t):
                dve.wait_ge(a_in[t], 16 * G)
                if t == TF:
                    dve.wait_ge(a_rest_in, 16 * len(a_rest))
                dve.wait_ge(pads_ready, 2)
                dve.wait_ge(columns_ready, 2)
                if t >= NT:
                    dve.wait_ge(at_ready, t - NT + 1)
                nc.vector.transpose(a_turned[:, t % NT, :, :].rearrange("p s (h r) -> p h s r", r=Q),
                                    a_nat[:, t, :, :].rearrange("p h (s c) -> p h s c", c=Q)).then_inc(at_turned, 1)

            dve.wait_ge(w_high, 1)
            nc.vector.tensor_tensor(w_pair[:, 2, 1, :], w_sb[:, 2, :], w_pair[:, 2, 0, :].bitcast(F32),
                                    ALU.subtract).then_inc(w_ready, 1)
            for i, (a, b) in enumerate(XG):
                dve.wait_ge(xt_high, i + 1)
                nc.vector.tensor_tensor(x_t[:, a:b, 1, :], in_bank(xt_ps[i], b - a), x_t[:, a:b, 0, :].bitcast(F32),
                                        ALU.subtract).then_inc(xt_ready, 1)
            turn_a(0)
            for i, (a, b) in enumerate(XG):
                dve.wait_ge(v0_high, i + 1)
                nc.vector.tensor_tensor(v[0][:, a:b, 1, :], in_bank(v0_ps[i], b - a), v[0][:, a:b, 0, :].bitcast(F32),
                                        ALU.subtract).then_inc(v0_ready, 1)
                if i == 0:
                    turn_a(1)
            for t in range(2, LEAD + 1):
                turn_a(t)

            def add_up(n):
                dve.wait_ge(mm_done, n + 1)
                if n >= SLOTS:
                    dve.wait_ge(low_ready, n - SLOTS + 1)
                nc.vector.tensor_reduce(u_sb[:, n % SLOTS, :], bank[bank_of(n)][:, 0:2 * F].rearrange("p (h f) -> p f h", h=2),
                                        AX.X, ALU.add).then_inc(sum_ready, 1)

            def check_low(k):
                i = dve_checks[k]
                nc.vector.tensor_reduce(low_sum[:, i:i + 1], low_words(i), AX.X, ALU.max).then_inc(lowsum_dve, 1)

            for n in range(2 * T):
                add_up(n)
                if n + LEAD + 1 < T:
                    turn_a(n + LEAD + 1)
                if 0 <= n - DVE_FROM < len(dve_checks) - DVE_LAST:
                    check_low(n - DVE_FROM)
            for k in range(len(dve_checks) - DVE_LAST, len(dve_checks)):
                check_low(k)

            def invert(n):
                t = n % T
                dve.wait_ge(std_ready, n + 1)
                nc.vector.reciprocal(rstd[:, t:t + 1], std[:, t:t + 1]).then_inc(rstd_ready, 1)

            def normalise(n):
                t = n % T
                dve.wait_ge(rstd_ready, n + 1)
                nc.vector.tensor_scalar(y_sb[:, t, :], y_sb[:, t, :], moments[:, t, 0:1], rstd[:, t:t + 1],
                                        ALU.subtract, ALU.mult).then_inc(y_ready, 1)

            def third_of_low(t):
                n = 2 * T + t
                dve.wait_ge(mm_done, n + 1)
                dve.wait_ge(sum_ready, n - SLOTS + 1)
                nc.vector.scalar_tensor_tensor(t_sb[:, n % SLOTS, :], bank[bank_of(n)][:, F:2 * F], 1.0 / 3.0, x_sb[:, t, :],
                                               ALU.mult, ALU.add).then_inc(part_ready, 1)

            def third_of_high(t):
                n = 2 * T + t
                dve.wait_ge(part_ready, t + 1)
                nc.vector.scalar_tensor_tensor(y_sb[:, t, :], bank[bank_of(n)][:, 0:F], 1.0 / 3.0, t_sb[:, n % SLOTS, :],
                                               ALU.mult, ALU.add).then_inc(sum_ready, 1)

            def take_stats(t):
                dve.wait_ge(sum_ready, 2 * T + t + 1)
                nc.vector.bn_stats(stats[:, t, :], y_sb[:, t, :]).then_inc(stats_ready, 1)

            def take_moments(t):
                dve.wait_ge(stats_ready, t + 1)
                nc.vector.bn_aggr(moments[:, t, :], stats[:, t, :]).then_inc(mom_ready, 1)

            for t in range(T - 1):
                third_of_low(t)
                if t >= 2:
                    invert(t - 2)
                if t >= 1:
                    take_stats(t - 1)
                third_of_high(t)
                if t >= 1:
                    take_moments(t - 1)
                if t >= 2:
                    normalise(t - 2)
                if 2 * T + t == verdict - 3:
                    dve.wait_ge(lowsum_act, len(act_checks))
                    dve.wait_ge(lowsum_dve, len(dve_checks))
                    nc.vector.tensor_reduce(low_all[:], low_sum[:], AX.X, ALU.add).then_inc(lowall_ready, 1)
                if 2 * T + t == verdict + 1:
                    dve.wait_ge(flag_done, 1)
                    nc.vector.tensor_scalar(flag[:], verdict_ps, 1.0, None, ALU.min
                                            ).then_inc(flag_ready, 1)

            third_of_low(T - 1)
            take_stats(T - 2)
            third_of_high(T - 1)
            take_moments(T - 2)
            invert(T - 3)
            take_stats(T - 1)
            normalise(T - 3)
            take_moments(T - 1)
            invert(T - 2)
            normalise(T - 2)
            invert(T - 1)
            normalise(T - 1)

            general = dve.value_load(flag[0:1, 0:1], min_val=0, max_val=1)
            with dve.If(general > 0):
                dve.wait_ge(sp_out_done, 16 * len(sp_out))
                dve.wait_ge(pool_out_done, 16 * len(pool_out))
                nc.vector.memset(low_all[:], 0.0).then_inc(g_sum, 1)
                for q in range(4):
                    with dve.Fori(0, T) as t:
                        m = q * T + t
                        if q < 3:
                            nc.vector.tensor_copy(g_xt[:, :, :], x_t[:, bass.ds(t, 1), :, :].rearrange(
                                "p o h n -> p (o h) n").bitcast(F32)).then_inc(g_x, 1)
                        if q >= 1:
                            nc.vector.tensor_copy(a_rows, a_nat[:, bass.ds(t, 1), :, :].rearrange("p o h j -> p (o h j)")
                                                  ).then_inc(g_rows, 1)
                            dve.wait_ge(g_rows, m - T + 1)
                            nc.vector.transpose(a_stage.rearrange("p s (h r) -> p h s r", r=Q),
                                                a_rows.rearrange("p (h s c) -> p h s c", h=G, c=Q)).then_inc(g_at, 1)
                        dve.wait_ge(g_mm, m + 1)
                        if q < 3:
                            nc.vector.tensor_copy(t_sb[:, 0, :], bank[0][:, F:2 * F]).then_inc(g_part, 1)
                            dve.wait_ge(g_part, m + 1)
                            nc.vector.tensor_tensor(g_factor[q % 2][:, bass.ds(t, 1), :].rearrange("p o f -> p (o f)"),
                                                    bank[0][:, 0:F], t_sb[:, 0, :], ALU.add).then_inc(g_sum, 1)
                        else:
                            nc.vector.scalar_tensor_tensor(y_sb[:, bass.ds(t, 1), :].rearrange("p o f -> p (o f)"),
                                                           bank[0][:, 0:F], 1.0 / 3.0,
                                                           x_sb[:, bass.ds(t, 1), :].rearrange("p o f -> p (o f)"),
                                                           ALU.mult, ALU.add).then_inc(g_sum, 1)
                dve.wait_ge(g_sum, 4 * T + 1)
                for t in range(T):
                    nc.vector.bn_stats(stats[:, t, :], y_sb[:, t, :]).then_inc(stats_ready, 1)
                    dve.wait_ge(stats_ready, T + t + 1)
                    nc.vector.bn_aggr(moments[:, t, :], stats[:, t, :]).then_inc(mom_ready, 1)
                    invert(T + t)
                    normalise(T + t)

        @block.tensor
        def _(pe):
            pe.wait_ge(warm_ready, 1)
            for i in range(WARM):
                nc.tensor.matmul(bank[4 + i % 4][:, :], warm[:, 0:P], warm[:, :], start=True, stop=True)
            pe.wait_ge(ident_ready, 2)
            pe.wait_ge(pads_ready, 1)
            pe.wait_ge(x_in, 16 * len(x_dmas))
            pe.wait_ge(x_rest_in, 16)

            for i, (a, b) in enumerate(XG):
                for k in range(a, b):
                    mm = nc.tensor.transpose(xt_ps[i][:, (k - a) * P:(k - a + 1) * P], x_sb[:, k, :], ident[:])
                mm.then_inc(xt_done, 1)

            def times_w(ps, t, w, stop):
                nc.tensor.matmul(ps, x_t[:, t, 0, :], w_pair[:, w, :, :].rearrange("p h f -> p (h f)"), start=True, stop=False)
                return nc.tensor.matmul(ps, x_t[:, t, 1, :], w_pair[:, w, :, :].rearrange("p h f -> p (h f)"),
                                        start=False, stop=stop)

            pe.wait_ge(w_ready, 1)
            for i, (a, b) in enumerate(XG):
                pe.wait_ge(xt_ready, i + 1)
                if i:
                    pe.wait_ge(xt_ready, 2)
                for t in range(a, b):
                    for h in range(4):
                        mm = nc.tensor.matmul(v0_ps[i][:, (t - a) * F:(t - a + 1) * F], x_t[:, t, h // 2, :],
                                              w_pair[:, 2, h % 2, :], start=(h == 0), stop=(h == 3))
                mm.then_inc(v0_done, 1)
            pe.wait_ge(w12_ready, 1)

            factor_waits = [0] * 3
            for n, s0, s1 in order:
                p, t = divmod(n, T)
                ps = bank[bank_of(n)][:, 0:2 * F]
                if s0 == -1:
                    if previous[n] is not None:
                        pe.wait_ge(sum_ready, previous[n] + 1)
                    elif n >= T:
                        pe.wait_ge(v0_ready, len(XG))
                    if p < 2:
                        times_w(ps, t, 1 - p, False)
                if p == 0 and s1 > 0:
                    pe.wait_ge(at_ready, t + 1)
                for s in range(max(s0, 0), s1):
                    if s >= factor_waits[p]:
                        factor_waits[p] = s + 1
                        if p == 0:
                            pe.wait_ge(v0_ready, s // XB + 1)
                        else:
                            pe.wait_ge(low_ready, (p - 1) * T + s + 1)
                    mm = nc.tensor.matmul(ps, a_t[:, t, s, :], v[p][:, s, :, :].rearrange("p h f -> p (h f)"),
                                          start=(p == 2 and s == 0), stop=(s == T - 1))
                if s1 == T:
                    mm.then_inc(mm_done, 1)
                if n == verdict:
                    pe.wait_ge(consts_ready, 2)
                    pe.wait_ge(lowall_ready, 1)
                    pe.wait_ge(sum_ready, 3 * T - 7)
                    nc.tensor.matmul(verdict_ps, low_all[:], ones[:],
                                     start=True, stop=True).then_inc(flag_done, 1)

            pe.wait_ge(flag_ready, 1)
            general = pe.value_load(flag[0:1, 0:1], min_val=0, max_val=1)
            with pe.If(general > 0):
                ps = bank[0]
                for q in range(4):
                    pe.wait_ge(g_sum, q * T + 1)
                    with pe.Fori(0, T) as t:
                        m = q * T + t
                        pe.wait_ge(g_sum, m + 1)
                        if q < 3:
                            pe.wait_ge(g_x, m + 1)
                            for h in range(2):
                                mm = nc.tensor.matmul(ps[:, 0:2 * F], g_xt[:, h, :],
                                                      w_pair[:, 2 - q, :, :].rearrange("p h f -> p (h f)"),
                                                      start=(h == 0), stop=(q == 0 and h == 1))
                        if q >= 1:
                            pe.wait_ge(g_at, m - T + 1)
                            for s in range(T):
                                mm = nc.tensor.matmul(ps[:, 0:F], a_stage[:, s, :], g_factor[(q - 1) % 2][:, s, :],
                                                      start=(q == 3 and s == 0), stop=(s == T - 1))
                        mm.then_inc(g_mm, 1)


_INS = ["x", "adj", "L0_gnn_W1", "L0_gnn_W2", "L0_gnn_W3"]


def kernel(**inputs):
    import numpy as _np
    import concourse.bacc as _bacc
    from concourse import mybir as _mybir
    from concourse.bass_utils import run_bass_kernel_spmd as _run

    nc = _bacc.Bacc("TRN2", target_bir_lowering=False, num_devices=1)
    arrays, args = {}, []
    for name in _INS:
        a = _np.ascontiguousarray(inputs[name])
        arrays[f"in_{name}_dram"] = a
        args.append(nc.dram_tensor(f"in_{name}_dram", a.shape, _mybir.dt.from_np(a.dtype), kind="ExternalInput").ap())
    shape = inputs["x"].shape
    args.append(nc.dram_tensor("out_0_dram", shape, _mybir.dt.float32, kind="ExternalOutput").ap())
    gnn_resnorm(nc, *args)
    r = _run(nc, [arrays], core_ids=[0])
    return r.results[0]["out_0_dram"]
```
